# Optimizing a Trainium2 kernel written in Bass

```python
import numpy as np
import jax
import jax.numpy as jnp

def _softmax(x, axis=-1):
    return jax.nn.softmax(x, axis=axis)

def _gelu(x):
    return jax.nn.gelu(x, approximate=True)

def _silu(x):
    return jax.nn.silu(x)

def _sigmoid(x):
    return jax.nn.sigmoid(x)

def _layernorm(x, axis=-1, eps=1e-05):
    m = jnp.mean(x, axis=axis, keepdims=True)
    v = jnp.var(x, axis=axis, keepdims=True)
    return (x - m) / jnp.sqrt(v + eps)

def _scatter_add(tgt, idx, src, axis=0):
    return tgt.at[idx].add(src)

def _segment_sum(src, seg, n):
    return jax.ops.segment_sum(src, seg, n)
kernel_name = 'mk_dlrm_tower_d1_rec_r8_ec299b'

def setup_inputs(seed: int=0):
    np.random.seed(seed)
    _w = jnp.asarray

    def _rec_inputs():
        import jax
        import jax.numpy as jnp
        _tk = jax.random.key(seed)
        ids = jnp.stack([jax.random.randint(jax.random.fold_in(_tk, 200 + f), (2048,), 0, v, jnp.int32) for f, v in enumerate([1250, 1250, 1250, 12500, 12500, 12500, 1000, 12500, 125000, 1000, 1000, 1250, 1000, 1250, 1000, 1000, 1000, 12500, 1000, 1250, 1250, 12500, 12500, 12500, 1000, 1000])], axis=1)
        tbl_0 = 0.05 * jax.random.normal(jax.random.fold_in(_tk, 500 + 0), (1250, 128), jnp.float32)
        tbl_1 = 0.05 * jax.random.normal(jax.random.fold_in(_tk, 500 + 1), (1250, 128), jnp.float32)
        tbl_2 = 0.05 * jax.random.normal(jax.random.fold_in(_tk, 500 + 2), (1250, 128), jnp.float32)
        tbl_3 = 0.05 * jax.random.normal(jax.random.fold_in(_tk, 500 + 3), (12500, 128), jnp.float32)
        tbl_4 = 0.05 * jax.random.normal(jax.random.fold_in(_tk, 500 + 4), (12500, 128), jnp.float32)
        tbl_5 = 0.05 * jax.random.normal(jax.random.fold_in(_tk, 500 + 5), (12500, 128), jnp.float32)
        tbl_6 = 0.05 * jax.random.normal(jax.random.fold_in(_tk, 500 + 6), (1000, 128), jnp.float32)
        tbl_7 = 0.05 * jax.random.normal(jax.random.fold_in(_tk, 500 + 7), (12500, 128), jnp.float32)
        tbl_8 = 0.05 * jax.random.normal(jax.random.fold_in(_tk, 500 + 8), (125000, 128), jnp.float32)
        tbl_9 = 0.05 * jax.random.normal(jax.random.fold_in(_tk, 500 + 9), (1000, 128), jnp.float32)
        tbl_10 = 0.05 * jax.random.normal(jax.random.fold_in(_tk, 500 + 10), (1000, 128), jnp.float32)
        tbl_11 = 0.05 * jax.random.normal(jax.random.fold_in(_tk, 500 + 11), (1250, 128), jnp.float32)
        tbl_12 = 0.05 * jax.random.normal(jax.random.fold_in(_tk, 500 + 12), (1000, 128), jnp.float32)
        tbl_13 = 0.05 * jax.random.normal(jax.random.fold_in(_tk, 500 + 13), (1250, 128), jnp.float32)
        tbl_14 = 0.05 * jax.random.normal(jax.random.fold_in(_tk, 500 + 14), (1000, 128), jnp.float32)
        tbl_15 = 0.05 * jax.random.normal(jax.random.fold_in(_tk, 500 + 15), (1000, 128), jnp.float32)
        tbl_16 = 0.05 * jax.random.normal(jax.random.fold_in(_tk, 500 + 16), (1000, 128), jnp.float32)
        tbl_17 = 0.05 * jax.random.normal(jax.random.fold_in(_tk, 500 + 17), (12500, 128), jnp.float32)
        tbl_18 = 0.05 * jax.random.normal(jax.random.fold_in(_tk, 500 + 18), (1000, 128), jnp.float32)
        tbl_19 = 0.05 * jax.random.normal(jax.random.fold_in(_tk, 500 + 19), (1250, 128), jnp.float32)
        tbl_20 = 0.05 * jax.random.normal(jax.random.fold_in(_tk, 500 + 20), (1250, 128), jnp.float32)
        tbl_21 = 0.05 * jax.random.normal(jax.random.fold_in(_tk, 500 + 21), (12500, 128), jnp.float32)
        tbl_22 = 0.05 * jax.random.normal(jax.random.fold_in(_tk, 500 + 22), (12500, 128), jnp.float32)
        tbl_23 = 0.05 * jax.random.normal(jax.random.fold_in(_tk, 500 + 23), (12500, 128), jnp.float32)
        tbl_24 = 0.05 * jax.random.normal(jax.random.fold_in(_tk, 500 + 24), (1000, 128), jnp.float32)
        tbl_25 = 0.05 * jax.random.normal(jax.random.fold_in(_tk, 500 + 25), (1000, 128), jnp.float32)
        _rk = jax.random.fold_in(_tk, 7)
        r_dense_features = -0.000520686 + 1.00062 * jax.random.normal(jax.random.fold_in(_rk, 101), (2048, 128), jnp.float32)
        W_top1 = 0.0405887 * jax.random.normal(jax.random.fold_in(_tk, 801), (607, 512), jnp.float32)
        W_top2 = 0.0441942 * jax.random.normal(jax.random.fold_in(_tk, 802), (512, 256), jnp.float32)
        W_top3 = 0.0625 * jax.random.normal(jax.random.fold_in(_tk, 803), (256, 1), jnp.float32)
        b_top1 = jnp.zeros((512,), jnp.float32)
        b_top2 = jnp.zeros((256,), jnp.float32)
        return (r_dense_features, ids, tbl_0, tbl_1, tbl_2, tbl_3, tbl_4, tbl_5, tbl_6, tbl_7, tbl_8, tbl_9, tbl_10, tbl_11, tbl_12, tbl_13, tbl_14, tbl_15, tbl_16, tbl_17, tbl_18, tbl_19, tbl_20, tbl_21, tbl_22, tbl_23, tbl_24, tbl_25, W_top1, b_top1, W_top2, b_top2, W_top3)
    r_dense_features, ids, tbl_0, tbl_1, tbl_2, tbl_3, tbl_4, tbl_5, tbl_6, tbl_7, tbl_8, tbl_9, tbl_10, tbl_11, tbl_12, tbl_13, tbl_14, tbl_15, tbl_16, tbl_17, tbl_18, tbl_19, tbl_20, tbl_21, tbl_22, tbl_23, tbl_24, tbl_25, W_top1, b_top1, W_top2, b_top2, W_top3 = _rec_inputs()

    def _L0_rec_setup():
        import jax, jax.numpy as jnp
        import numpy as np
        B, F, D = (2048, 26, 128)
        key = jax.random.key(seed)
        k1, k2 = jax.random.split(key)
        dense_features = jax.random.normal(k1, (B, D), dtype=jnp.float32)
        sparse_values = jax.random.normal(k2, (B, F, D), dtype=jnp.float32)
        return {'dense_features': dense_features, 'sparse_values': sparse_values}
    _L0_rec_all = _L0_rec_setup()
    _L0_rec_in = {k: v for k, v in _L0_rec_all.items() if k in ()}
    del _L0_rec_all
    return {'r_dense_features': r_dense_features, 'ids': ids, 'tbl_0': tbl_0, 'tbl_1': tbl_1, 'tbl_2': tbl_2, 'tbl_3': tbl_3, 'tbl_4': tbl_4, 'tbl_5': tbl_5, 'tbl_6': tbl_6, 'tbl_7': tbl_7, 'tbl_8': tbl_8, 'tbl_9': tbl_9, 'tbl_10': tbl_10, 'tbl_11': tbl_11, 'tbl_12': tbl_12, 'tbl_13': tbl_13, 'tbl_14': tbl_14, 'tbl_15': tbl_15, 'tbl_16': tbl_16, 'tbl_17': tbl_17, 'tbl_18': tbl_18, 'tbl_19': tbl_19, 'tbl_20': tbl_20, 'tbl_21': tbl_21, 'tbl_22': tbl_22, 'tbl_23': tbl_23, 'tbl_24': tbl_24, 'tbl_25': tbl_25, 'W_top1': W_top1, 'b_top1': b_top1, 'W_top2': W_top2, 'b_top2': b_top2, 'W_top3': W_top3}

def reference(r_dense_features, ids, tbl_0, tbl_1, tbl_2, tbl_3, tbl_4, tbl_5, tbl_6, tbl_7, tbl_8, tbl_9, tbl_10, tbl_11, tbl_12, tbl_13, tbl_14, tbl_15, tbl_16, tbl_17, tbl_18, tbl_19, tbl_20, tbl_21, tbl_22, tbl_23, tbl_24, tbl_25, W_top1, b_top1, W_top2, b_top2, W_top3):
    import jax
    import jax.numpy as jnp

    def _L0_rec_ref(dense_features, sparse_values):
        import jax, jax.numpy as jnp
        import numpy as np
        B, F, D = (2048, 26, 128)
        sd = jnp.einsum('bfd,bd->bf', sparse_values, dense_features)
        ss = jnp.einsum('bfd,bgd->bfg', sparse_values, sparse_values)
        iu, ju = jnp.triu_indices(F, k=1)
        pairs = ss[:, iu, ju]
        return jnp.concatenate([dense_features, sd, pairs], axis=1)
    e = jnp.stack([tbl_0[ids[:, 0]], tbl_1[ids[:, 1]], tbl_2[ids[:, 2]], tbl_3[ids[:, 3]], tbl_4[ids[:, 4]], tbl_5[ids[:, 5]], tbl_6[ids[:, 6]], tbl_7[ids[:, 7]], tbl_8[ids[:, 8]], tbl_9[ids[:, 9]], tbl_10[ids[:, 10]], tbl_11[ids[:, 11]], tbl_12[ids[:, 12]], tbl_13[ids[:, 13]], tbl_14[ids[:, 14]], tbl_15[ids[:, 15]], tbl_16[ids[:, 16]], tbl_17[ids[:, 17]], tbl_18[ids[:, 18]], tbl_19[ids[:, 19]], tbl_20[ids[:, 20]], tbl_21[ids[:, 21]], tbl_22[ids[:, 22]], tbl_23[ids[:, 23]], tbl_24[ids[:, 24]], tbl_25[ids[:, 25]]], axis=1)
    z = _L0_rec_ref(r_dense_features, e)
    z = z.reshape(z.shape[0], -1)
    h = jnp.concatenate([z, r_dense_features], axis=1)
    h = jnp.maximum(h @ W_top1 + b_top1, 0.0)
    h = jnp.maximum(h @ W_top2 + b_top2, 0.0)
    y = h @ W_top3
    return y

_drawn_inputs = setup_inputs


def setup_inputs(seed=0):
    import zlib

    import numpy as np

    out = dict(_drawn_inputs(seed))
    spreads = {'b_top1': (0.0, 0.1), 'b_top2': (0.0, 0.1)}
    factors = {}
    for name, (base, spread) in spreads.items():
        noise = np.random.default_rng([zlib.crc32(name.encode()), seed]).standard_normal(out[name].shape)
        drawn = base * np.exp(spread * noise) if base else spread * noise
        out[name] = jnp.asarray(drawn.astype(out[name].dtype))
    for name, factor in factors.items():
        out[name] = (out[name] * factor).astype(out[name].dtype)
    return out
```

```python
from contextlib import ExitStack

import numpy as np

import concourse.bass as bass
from concourse import mybir

P = 128
QUAD = 32
TILES_PER_PAIR = 2
CHUNK = 4
GROUP = 4
GROUPS_PER_UNIT = 16


def dlrm_tower(nc, table, dense, ids, W1, b1, W2, b2, W3, out):
    fp32, int32 = mybir.dt.float32, mybir.dt.int32
    ALU, ACT = mybir.AluOpType, mybir.ActivationFunctionType

    B, F = ids.shape
    D = dense.shape[1]
    N1, N2 = W2.shape
    V = F + 1
    KT = -(-F // 4)
    last_rows = (F - 4 * (KT - 1)) * QUAD
    PAIRS = B // (P * TILES_PER_PAIR)
    NS = P * TILES_PER_PAIR
    UNITS = P // (GROUP * GROUPS_PER_UNIT)
    CHUNKS = -(-V // CHUNK)
    C1, C2 = N1 // P, N2 // P
    first_pair_row = D + F
    last_dense_row = first_pair_row + F * (F - 1) // 2
    DMA = 16
    evacs = [(CHUNKS + 1) // 2, CHUNKS // 2]

    with ExitStack() as ctx:
        def sb(name, shape, dt=fp32):
            return ctx.enter_context(nc.sbuf_tensor(name, shape, dt))

        def sem(name):
            return ctx.enter_context(nc.semaphore(name))

        ids_sb = sb("ids_sb", [P, TILES_PER_PAIR, F], int32)
        rows = sb("rows", [P, TILES_PER_PAIR, V, D])
        vecs_t = sb("vecs_t", [D, TILES_PER_PAIR, P, QUAD])
        dense_t = sb("dense_t", [D, NS])
        dots = sb("dots", [P, KT, NS])
        h1 = sb("h1", [P, C1, NS])
        h2 = sb("h2", [P, C2, NS])
        y = sb("y", [1, B])
        w_dots = sb("w_dots", [P, KT, N1])
        w_dense = sb("w_dense", [D, 2, N1])
        w2 = sb("w2", [P, C1, N2])
        w3 = sb("w3", [P, C2])
        bias1 = sb("bias1", [P, C1])
        bias2 = sb("bias2", [P, C2])
        ident = sb("ident", [P, P])

        chunk_ps = [ctx.enter_context(nc.psum_tensor(f"chunk_ps{b}", [P, CHUNK, P], fp32)) for b in range(2)]
        gram_ps = ctx.enter_context(nc.psum_tensor("gram_ps", [P, GROUPS_PER_UNIT, P], fp32))
        mlp_ps = [ctx.enter_context(nc.psum_tensor(f"mlp_ps{b}", [P, 2, NS], fp32)) for b in range(2)]

        ids_landed = [sem(f"ids_landed{h}") for h in range(TILES_PER_PAIR)]
        dense_landed = [sem(f"dense_landed{h}") for h in range(TILES_PER_PAIR)]
        rows_landed = [sem(f"rows_landed{h}") for h in range(TILES_PER_PAIR)]
        gathers_begun = sem("gathers_begun")
        weights_landed = sem("weights_landed")
        w_dots_zeroed = sem("w_dots_zeroed")
        w_dense_landed = sem("w_dense_landed")
        w_dense_summed = sem("w_dense_summed")
        ident_zeroed = sem("ident_zeroed")
        ident_ready = sem("ident_ready")
        pads_zeroed = sem("pads_zeroed")
        transposed = [sem(f"transposed{b}") for b in range(2)]
        chunk_moved = [sem(f"chunk_moved{b}") for b in range(2)]
        gram_ready = sem("gram_ready")
        dots_moved = [sem(f"dots_moved{e}") for e in range(2)]
        layer1_ready = [sem(f"layer1_ready{b}") for b in range(2)]
        h1_ready = [sem(f"h1_ready{b}") for b in range(2)]
        layer2_ready = [sem(f"layer2_ready{b}") for b in range(2)]
        h2_ready = [sem(f"h2_ready{b}") for b in range(2)]
        y_ps_ready = sem("y_ps_ready")
        y_moved = sem("y_moved")
        out_written = sem("out_written")

        ids_of = ids.rearrange("(i h p) f -> i h p f", h=TILES_PER_PAIR, p=P)
        dense_of = dense.rearrange("(i h p) d -> i h p d", h=TILES_PER_PAIR, p=P)

        def slot_used(i, h):
            return (i * TILES_PER_PAIR + h - TILES_PER_PAIR + 1) * evacs[0]

        def move_chunk(engine_copy, b, c, h):
            n = min(CHUNK, V - CHUNK * c)
            if c == CHUNKS - 1:
                engine_copy(dense_t[:, h * P:(h + 1) * P], chunk_ps[b][:, n - 1, :])
            return engine_copy(vecs_t[:, h, :, CHUNK * c:CHUNK * c + n].rearrange("d s v -> d v s"),
                               chunk_ps[b][:, 0:n, :])

        def move_dots(engine_copy, blocks, h, u):
            at = h * P + u * GROUP * GROUPS_PER_UNIT
            for s in blocks:
                for q in range(4):
                    n = len(range(q, F, 4))
                    last = engine_copy(
                        dots[q * QUAD:(q + 1) * QUAD, 0:n, at + s:at + GROUP * GROUPS_PER_UNIT:GROUP]
                        .rearrange("f k g -> f g k"),
                        gram_ps[s * QUAD:(s + 1) * QUAD, :, s * F + q:(s + 1) * F:4])
            return last

        block = ctx.enter_context(nc.Block())

        @block.sync
        def _(sp):
            for h in range(TILES_PER_PAIR):
                sp.dma_start(ids_sb[:, h, :], ids_of[0, h]).then_inc(ids_landed[h], DMA)
                sp.dma_start(rows[:, h, F, :], dense_of[0, h]).then_inc(dense_landed[h], DMA)
            with sp.Fori(1, PAIRS) as i:
                for h in range(TILES_PER_PAIR):
                    sp.wait_ge(rows_landed[h], i * (F * DMA))
                    sp.dma_start(ids_sb[:, h, :], ids_of[bass.ds(i, 1), h].rearrange("o p f -> (o p) f")).then_inc(ids_landed[h], DMA)
                    sp.wait_ge(transposed[0], slot_used(i, h))
                    sp.dma_start(rows[:, h, F, :], dense_of[bass.ds(i, 1), h].rearrange("o p d -> (o p) d")).then_inc(dense_landed[h], DMA)
            sp.wait_ge(y_moved, PAIRS)
            sp.dma_start(out.rearrange("b o -> o b"), y[:], allow_slow_non_contiguous=True).then_inc(out_written, DMA)
            sp.wait_ge(out_written, DMA)

        @block.gpsimd
        def _(pool):
            nc.gpsimd.memset(ident[:], 0.0).then_inc(ident_zeroed, 1)
            pool.wait_ge(ident_zeroed, 1)
            nc.gpsimd.affine_select(out=ident[:], in_=ident[:], compare_op=ALU.not_equal, fill=1.0,
                                    base=0, pattern=[[-1, P]], channel_multiplier=1).then_inc(ident_ready, 1)

            def gather(h):
                for f in range(F):
                    nc.gpsimd.indirect_dma_start(
                        out=rows[:, h, f, :], out_offset=None, in_=table[f],
                        in_offset=bass.IndirectOffsetOnAxis(ap=ids_sb[:, h, f:f + 1], axis=0),
                    ).then_inc(rows_landed[h], DMA)

            for h in range(TILES_PER_PAIR):
                pool.wait_ge(ids_landed[h], DMA)
                gather(h)
            with pool.Fori(1, PAIRS) as i:
                for h in range(TILES_PER_PAIR):
                    pool.wait_ge(ids_landed[h], (i + 1) * DMA)
                    pool.wait_ge(transposed[0], slot_used(i, h))
                    pool.sem_inc(gathers_begun, 1)
                    gather(h)

        @block.scalar
        def _(act):
            def copy(out_ap, in_ap):
                return nc.scalar.activation(out_ap, in_ap, ACT.Copy)

            act.dma_start(w_dense[:, 0, :], W1[0:D, :]).then_inc(w_dense_landed, DMA)
            act.dma_start(w_dense[:, 1, :], W1[last_dense_row:last_dense_row + D, :]).then_inc(w_dense_landed, DMA)
            act.dma_start(w2[:], W2.rearrange("(c p) n -> p c n", p=P)).then_inc(weights_landed, DMA)
            act.dma_start(w3[:], W3.rearrange("(c p) o -> p (c o)", p=P), allow_slow_non_contiguous=True).then_inc(weights_landed, DMA)
            act.dma_start(bias1[:], b1.rearrange("(c p) -> p c", p=P), allow_slow_non_contiguous=True).then_inc(weights_landed, DMA)
            act.dma_start(bias2[:], b2.rearrange("(c p) -> p c", p=P), allow_slow_non_contiguous=True).then_inc(weights_landed, DMA)
            act.wait_ge(w_dots_zeroed, 1)
            row = first_pair_row
            for g in range(F - 1):
                at, n = (g % 4) * QUAD, F - 1 - g
                act.dma_start(w_dots[at + g + 1:at + F, g // 4, :], W1[row:row + n, :]).then_inc(weights_landed, DMA)
                row += n
            for q in range(4):
                at, n = q * QUAD + F, len(range(q, F, 4))
                act.dma_start(w_dots[at:at + 1, 0:n, :],
                              W1[D + q:D + F:4, :].rearrange("(o k) n -> o k n", o=1)).then_inc(weights_landed, DMA)

            with act.Fori(0, PAIRS) as i:
                for h in range(TILES_PER_PAIR):
                    for c in range(1, CHUNKS, 2):
                        act.wait_ge(transposed[1], (i * TILES_PER_PAIR + h) * evacs[1] + c // 2 + 1)
                        move_chunk(copy, 1, c, h).then_inc(chunk_moved[1], 1)
                    for u in range(UNITS):
                        act.wait_ge(gram_ready, (i * TILES_PER_PAIR + h) * UNITS + u + 1)
                        move_dots(copy, (2, 3), h, u).then_inc(dots_moved[1], 1)
                act.wait_ge(layer1_ready[1], i + 1)
                for c in range(2, 4):
                    last = nc.scalar.activation(h1[:, c, :], mlp_ps[1][:, c - 2, :], ACT.Relu, bias=bias1[:, c:c + 1])
                last.then_inc(h1_ready[1], 1)
                act.wait_ge(layer2_ready[1], i + 1)
                nc.scalar.activation(h2[:, 1, :], mlp_ps[1][:, 0, :], ACT.Relu, bias=bias2[:, 1:2]).then_inc(h2_ready[1], 1)

        @block.vector
        def _(dve):
            nc.vector.memset(w_dots[:], 0.0).then_inc(w_dots_zeroed, 1)
            nc.vector.memset(vecs_t[:, :, :, V:QUAD], 0.0).then_inc(pads_zeroed, 1)
            dve.wait_ge(w_dense_landed, 2 * DMA)
            nc.vector.tensor_tensor(w_dense[:, 0, :], w_dense[:, 0, :], w_dense[:, 1, :], ALU.add).then_inc(w_dense_summed, 1)
            dve.wait_ge(weights_landed, (4 + F - 1 + 4) * DMA)

            with dve.Fori(0, PAIRS) as i:
                for h in range(TILES_PER_PAIR):
                    for c in range(0, CHUNKS, 2):
                        dve.wait_ge(transposed[0], (i * TILES_PER_PAIR + h) * evacs[0] + c // 2 + 1)
                        move_chunk(nc.vector.tensor_copy, 0, c, h).then_inc(chunk_moved[0], 1)
                    for u in range(UNITS):
                        dve.wait_ge(gram_ready, (i * TILES_PER_PAIR + h) * UNITS + u + 1)
                        move_dots(nc.vector.tensor_copy, (0, 1), h, u).then_inc(dots_moved[0], 1)
                dve.wait_ge(layer1_ready[0], i + 1)
                for c in range(2):
                    last = nc.vector.tensor_scalar(h1[:, c, :], mlp_ps[0][:, c, :], bias1[:, c:c + 1], 0.0, ALU.add, ALU.max)
                last.then_inc(h1_ready[0], 1)
                dve.wait_ge(layer2_ready[0], i + 1)
                nc.vector.tensor_scalar(h2[:, 0, :], mlp_ps[0][:, 0, :], bias2[:, 0:1], 0.0, ALU.add, ALU.max).then_inc(h2_ready[0], 1)
                dve.wait_ge(y_ps_ready, i + 1)
                nc.vector.tensor_scalar(y[:, bass.ds(i * NS, NS)], mlp_ps[0][0:1, 1, :], 1.0, None, ALU.mult).then_inc(y_moved, 1)

        @block.tensor
        def _(pe):
            pe.wait_ge(ident_ready, 1)
            pe.wait_ge(pads_zeroed, 1)
            pe.wait_ge(w_dense_summed, 1)
            pe.wait_ge(weights_landed, (4 + F - 1 + 4) * DMA)
            with pe.Fori(0, PAIRS) as i:
                for h in range(TILES_PER_PAIR):
                    tile = i * TILES_PER_PAIR + h
                    pe.wait_ge(rows_landed[h], (i + 1) * (F * DMA))
                    pe.wait_ge(dense_landed[h], (i + 1) * DMA)
                    for c in range(CHUNKS):
                        b = c % 2
                        if c >= 2:
                            pe.wait_ge(chunk_moved[b], tile * evacs[b] + c // 2)
                        for v in range(CHUNK * c, min(V, CHUNK * (c + 1))):
                            last = nc.tensor.transpose(chunk_ps[b][:, v - CHUNK * c, :], rows[:, h, v, :], ident[:])
                        last.then_inc(transposed[b], 1)
                    for b in range(2):
                        pe.wait_ge(chunk_moved[b], tile * evacs[b] + evacs[b])
                    for u in range(UNITS):
                        if (h, u) != (0, 0):
                            for e in range(2):
                                pe.wait_ge(dots_moved[e], tile * UNITS + u)
                        for n in range(GROUPS_PER_UNIT):
                            at = (u * GROUPS_PER_UNIT + n) * GROUP
                            last = nc.tensor.matmul(
                                gram_ps[:, n, 0:GROUP * F].rearrange("p (s g) -> p s g", s=GROUP),
                                vecs_t[:, h, at:at + GROUP, :].rearrange("d s v -> d (s v)"),
                                vecs_t[:, h, at:at + GROUP, 0:F], start=True, stop=True)
                        last.then_inc(gram_ready, 1)
                for e in range(2):
                    pe.wait_ge(dots_moved[e], (i + 1) * (TILES_PER_PAIR * UNITS))
                for c in range(C1):
                    to, cols = mlp_ps[c // 2][:, c % 2, :], slice(c * P, (c + 1) * P)
                    nc.tensor.matmul(to, w_dense[:, 0, cols], dense_t[:], start=True, stop=False)
                    for k in range(KT):
                        n = last_rows if k == KT - 1 else P
                        last = nc.tensor.matmul(to, w_dots[0:n, k, cols], dots[0:n, k, :], start=False, stop=(k == KT - 1))
                    if c % 2:
                        last.then_inc(layer1_ready[c // 2], 1)
                for b in range(2):
                    pe.wait_ge(h1_ready[b], i + 1)
                for m in range(C2):
                    for c in range(C1):
                        last = nc.tensor.matmul(mlp_ps[m][:, 0, :], w2[:, c, m * P:(m + 1) * P], h1[:, c, :],
                                                start=(c == 0), stop=(c == C1 - 1))
                    last.then_inc(layer2_ready[m], 1)
                for b in range(2):
                    pe.wait_ge(h2_ready[b], i + 1)
                for m in range(C2):
                    last = nc.tensor.matmul(mlp_ps[0][0:1, 1, :], w3[:, m:m + 1], h2[:, m, :],
                                            start=(m == 0), stop=(m == C2 - 1))
                last.then_inc(y_ps_ready, 1)


def kernel(**inputs):
    import concourse.bacc as bacc
    from concourse.bass_utils import run_bass_kernel_spmd

    nc = bacc.Bacc("TRN2", target_bir_lowering=False, num_devices=1)
    arrays, aps = {}, {}
    for name, a in inputs.items():
        a = np.ascontiguousarray(a)
        arrays[f"in_{name}"] = a
        aps[name] = nc.dram_tensor(f"in_{name}", a.shape, mybir.dt.from_np(a.dtype), kind="ExternalInput").ap()
    B, F = inputs["ids"].shape
    out = nc.dram_tensor("out_y", (B, 1), mybir.dt.float32, kind="ExternalOutput").ap()
    dlrm_tower(nc, [aps[f"tbl_{f}"] for f in range(F)], aps["r_dense_features"], aps["ids"],
               aps["W_top1"], aps["b_top1"], aps["W_top2"], aps["b_top2"], aps["W_top3"], out)
    return run_bass_kernel_spmd(nc, [arrays], core_ids=[0]).results[0]["out_y"]
```

```python
from contextlib import ExitStack

import numpy as np

import concourse.bass as bass
from concourse import mybir

P = 128
QUAD = 32
TILES = 2
CHUNK = 4
GROUP = 4
GROUPS_PER_UNIT = 16
ROWS_AT_MOST = 1024
SLOTS = 4
ON_CHIP = (14, 15, 16, 24, 25)
DMA = 16
CHUNK_VECTORS = [[0, 1, 2, 3], [4, 5, 6, 7], [8, 9, 10, 11], [17, 18, 19, 20], [21, 22, 23], [12, 13, 26]]
DOT_BLOCKS = {0: (0, 1), 1: (2, 3)}
STEPS = [("transpose 0", 0), ("transpose 0", 1), ("split", 1), ("look up", 0), ("look up", 1), ("layer 1", 0), ("transpose 0", 2),
         ("look up", 2), ("layer 1", 1), ("transpose 0", 3), ("look up", 3), ("transpose 0", 4), ("look up", 4),
         ("transpose 0", 5), ("layer 1", 2), ("gram", 0), ("layer 1", 3),
         ("transpose 1", 0), ("transpose 1", 1), ("gram", 1), ("transpose 1", 2), ("transpose 1", 3), ("layer 2", 0), ("split", 0),
         ("transpose 1", 4), ("transpose 1", 5), ("layer 2", 1), ("gram", 2), ("layer 3", 0), ("gram", 3)]
SPLIT_WEIGHTS_AFTER = ("transpose 0", 5)
BUILD_AHEAD = {("transpose 1", 5): 0, ("layer 3", 0): 1}


def runs_of(vectors):
    runs = []
    for n, v in enumerate(vectors):
        if runs and v == runs[-1][0] + runs[-1][1]:
            runs[-1][1] += 1
        else:
            runs.append([v, 1, n])
    return runs


def dlrm_tower(nc, table, dense, ids, ids_t, W1, b1, W2, b2, W3, out):
    fp32, fp32r, int32 = mybir.dt.float32, mybir.dt.float32r, mybir.dt.int32
    ALU, ACT = mybir.AluOpType, mybir.ActivationFunctionType

    B, F = ids.shape
    D = dense.shape[1]
    N1, N2 = W2.shape
    V = F + 1
    KT = -(-F // 4)
    last_rows = (F - 4 * (KT - 1)) * QUAD
    NS = P * TILES
    PAIRS = B // NS
    UNITS = P // (GROUP * GROUPS_PER_UNIT)
    C1, C2 = N1 // P, N2 // P
    first_pair_row = D + F
    last_dense_row = first_pair_row + F * (F - 1) // 2
    WEIGHT_DMAS = 6 + (F - 1) + 4

    gathered = [f for f in range(F) if f not in ON_CHIP]
    sources = gathered + [F]
    G, X = len(gathered), len(ON_CHIP)
    TR = table[ON_CHIP[0]].shape[0]
    M = ROWS_AT_MOST // P
    TP = TR // M
    assert all(table[f].shape[0] == TR for f in ON_CHIP) and TP * M == TR

    CHUNKS = len(CHUNK_VECTORS)
    assert sorted(sum(CHUNK_VECTORS, [])) == sources
    fills = [step for step in STEPS if step[0] in ("look up", "transpose 0", "transpose 1")]
    FILLS = len(fills)
    assert FILLS == X + 2 * CHUNKS

    def fill_no(p, kind, n):
        at = p * FILLS + fills.index((kind, n))
        return at % 2, at // 2

    def last_fill(p, h, b):
        kinds = (f"transpose {h}", "look up")
        return max(fill_no(p, *fill)[1] for fill in fills if fill[0] in kinds and fill_no(p, *fill)[0] == b)

    with ExitStack() as ctx:
        def sb(name, shape, dt=fp32):
            return ctx.enter_context(nc.sbuf_tensor(name, shape, dt))

        def sem(name):
            return ctx.enter_context(nc.semaphore(name))

        ids_sb = sb("ids_sb", [P, SLOTS, F], int32)
        rows = sb("rows", [P, SLOTS, G, D])
        dense_rows = sb("dense_rows", [P, TILES, D])
        ids_wide = sb("ids_wide", [TP, X, NS], int32)
        row_id = sb("row_id", [TP, M], int32)
        onehot = sb("onehot", [TP, 2, M, NS], fp32r)
        table_hi = sb("table_hi", [TP, X, M, D], fp32r)
        table_lo = sb("table_lo", [TP, X, M, D], fp32r)
        vecs = sb("vecs", [D, NS, QUAD])
        dots = sb("dots", [P, KT + 1, NS])
        dots_hi = sb("dots_hi", [P, KT + 1, NS], fp32r)
        dots_lo = sb("dots_lo", [P, KT + 1, NS], fp32r)
        h1 = sb("h1", [P, C1, NS])
        h2 = sb("h2", [P, C2, NS])
        y = sb("y", [QUAD + 1, PAIRS // 2, NS])
        w1_hi = sb("w1_hi", [P, KT + 1, N1], fp32r)
        w1_lo = sb("w1_lo", [P, KT + 1, N1], fp32r)
        w2 = sb("w2", [P, C1, N2])
        w3 = sb("w3", [P, C2])
        bias1 = sb("bias1", [P, C1])
        bias2 = sb("bias2", [P, C2])
        ident = sb("ident", [P, P])
        staging = [dots[0:TP].rearrange("p k s -> p (k s)")[:, s * M * D:(s + 1) * M * D] for s in range(2)]
        w1 = rows[:, 2:4].rearrange("p s g d -> p (s g d)")[:, 0:(KT + 2) * N1].rearrange("p (k n) -> p k n", n=N1)

        fill_ps = [ctx.enter_context(nc.psum_tensor(f"fill_ps{b}", [P, CHUNK, P], fp32)) for b in range(2)]
        gram_ps = ctx.enter_context(nc.psum_tensor("gram_ps", [P, GROUPS_PER_UNIT, P], fp32))
        mlp_ps = [ctx.enter_context(nc.psum_tensor(f"mlp_ps{b}", [P, 2, NS], fp32)) for b in range(2)]
        looked_up = [fill_ps[b][:].rearrange("d v s -> d (v s)")[:, 0:NS] for b in range(2)]

        ids_landed = [sem(f"ids_landed{s}") for s in range(SLOTS)]
        dense_landed = [sem(f"dense_landed{h}") for h in range(TILES)]
        rows_landed = [sem(f"rows_landed{s}") for s in range(SLOTS)]
        gathers_begun = sem("gathers_begun")
        ids_wide_landed = sem("ids_wide_landed")
        table_landed = [sem(f"table_landed{s}") for s in range(2)]
        table_hi_ready = sem("table_hi_ready")
        table_lo_ready = sem("table_lo_ready")
        weights_landed = sem("weights_landed")
        w1_zeroed = sem("w1_zeroed")
        w1_summed = sem("w1_summed")
        w1_hi_ready = sem("w1_hi_ready")
        w1_lo_ready = sem("w1_lo_ready")
        ident_zeroed = sem("ident_zeroed")
        ident_ready = sem("ident_ready")
        row_id_ready = sem("row_id_ready")
        pads_zeroed = sem("pads_zeroed")
        onehot_ready = sem("onehot_ready")
        filled = [sem(f"filled{b}") for b in range(2)]
        moved = [sem(f"moved{b}") for b in range(2)]
        gram_ready = sem("gram_ready")
        dots_moved = [sem(f"dots_moved{e}") for e in range(2)]
        split_hi = sem("split_hi")
        split_lo = sem("split_lo")
        dots_padded = sem("dots_padded")
        layer1_ready = sem("layer1_ready")
        h1_ready = sem("h1_ready")
        layer2_ready = sem("layer2_ready")
        h2_ready = sem("h2_ready")
        y_ps_ready = sem("y_ps_ready")
        y_moved = sem("y_moved")
        out_written = sem("out_written")

        ids_of = ids.rearrange("(q s p) f -> q s p f", s=SLOTS, p=P)
        dense_of = dense.rearrange("(i h p) d -> i h p d", h=TILES, p=P)

        def run_pairs(engine, pair):
            pair(0, 0, first=True)
            with engine.Fori(0, PAIRS // 2 - 1) as q:
                pair(q, 1)
                pair(q + 1, 0)
            pair(PAIRS // 2 - 1, 1, last=True)

        def before(q, p):
            return (q, 0) if p else (q - 1, 1)

        def after(q, p):
            return (q + 1, 0) if p else (q, 1)

        def move_fill(copy, b, kind, n):
            if kind == "look up":
                return copy(vecs[:, :, ON_CHIP[n]], looked_up[b])
            h = int(kind[-1])
            for f, m, at in runs_of(CHUNK_VECTORS[n]):
                last = copy(vecs[:, h * P:(h + 1) * P, f:f + m].rearrange("d s v -> d v s"), fill_ps[b][:, at:at + m, :])
                if f + m == V:
                    last = copy(dots[:, KT, h * P:(h + 1) * P], fill_ps[b][:, at + m - 1, :])
            return last

        def move_dots(copy, blocks, h, u):
            at = h * P + u * GROUP * GROUPS_PER_UNIT
            for s in blocks:
                for r in range(4):
                    n = len(range(r, F, 4))
                    last = copy(
                        dots[r * QUAD:(r + 1) * QUAD, 0:n, at + s:at + GROUP * GROUPS_PER_UNIT:GROUP]
                        .rearrange("f k g -> f g k"),
                        gram_ps[s * QUAD:(s + 1) * QUAD, :, s * F + r:(s + 1) * F:4])
            return last

        block = ctx.enter_context(nc.Block())

        @block.sync
        def _(sp):
            for s in range(SLOTS):
                sp.dma_start(ids_sb[:, s, :], ids_of[0, s]).then_inc(ids_landed[s], DMA)
                if s < TILES:
                    sp.dma_start(dense_rows[:, s, :], dense_of[0, s]).then_inc(dense_landed[s], DMA)
                if s < 2:
                    sp.dma_start(staging[s], table[ON_CHIP[s]].rearrange("(p m) d -> p (m d)", m=M)).then_inc(table_landed[s], DMA)
            sp.dma_start(ids_wide[:], ids_t[:, 0:NS].partition_broadcast(TP)).then_inc(ids_wide_landed, DMA)
            for x in range(2, X):
                sp.wait_ge(table_lo_ready, x - 1)
                sp.dma_start(staging[x % 2], table[ON_CHIP[x]].rearrange("(p m) d -> p (m d)", m=M)).then_inc(table_landed[x % 2], DMA)

            sp.dma_start(w1[:, KT, :], W1[0:D, :]).then_inc(weights_landed, DMA)
            sp.dma_start(w1[:, KT + 1, :], W1[last_dense_row:last_dense_row + D, :]).then_inc(weights_landed, DMA)
            sp.dma_start(w2[:], W2.rearrange("(c p) n -> p c n", p=P)).then_inc(weights_landed, DMA)
            sp.dma_start(w3[:], W3.rearrange("(c p) o -> p (c o)", p=P), allow_slow_non_contiguous=True).then_inc(weights_landed, DMA)
            sp.dma_start(bias1[:], b1.rearrange("(c p) -> p c", p=P), allow_slow_non_contiguous=True).then_inc(weights_landed, DMA)
            sp.dma_start(bias2[:], b2.rearrange("(c p) -> p c", p=P), allow_slow_non_contiguous=True).then_inc(weights_landed, DMA)
            sp.wait_ge(w1_zeroed, 1)
            row = first_pair_row
            for g in range(F - 1):
                at, n = (g % 4) * QUAD, F - 1 - g
                sp.dma_start(w1[at + g + 1:at + F, g // 4, :], W1[row:row + n, :]).then_inc(weights_landed, DMA)
                row += n
            for r in range(4):
                at, n = r * QUAD + F, len(range(r, F, 4))
                sp.dma_start(w1[at:at + 1, 0:n, :],
                              W1[D + r:D + F:4, :].rearrange("(o k) n -> o k n", o=1)).then_inc(weights_landed, DMA)

            def load_pair(i, p, q_of_slots):
                if q_of_slots is not None:
                    for s in (2 * p, 2 * p + 1):
                        sp.wait_ge(rows_landed[s], q_of_slots * (G * DMA))
                        sp.dma_start(ids_sb[:, s, :], ids_of[bass.ds(q_of_slots, 1), s].rearrange("o p f -> (o p) f")).then_inc(ids_landed[s], DMA)
                sp.wait_ge(onehot_ready, i * X)
                cols = ids_t[:, i * NS:(i + 1) * NS] if isinstance(i, int) else ids_t[:, bass.ds(i * NS, NS)]
                sp.dma_start(ids_wide[:], cols.partition_broadcast(TP)).then_inc(ids_wide_landed, DMA)
                for h in range(TILES):
                    (q, pp) = (0, 0) if isinstance(i, int) else before(q_of_slots, p)
                    b, no = fill_no(pp, f"transpose {h}", CHUNKS - 1)
                    sp.wait_ge(filled[b], q * FILLS + (no + 1))
                    tile = dense_of[i, h] if isinstance(i, int) else dense_of[bass.ds(i, 1), h].rearrange("o p d -> (o p) d")
                    sp.dma_start(dense_rows[:, h, :], tile).then_inc(dense_landed[h], DMA)

            load_pair(1, 1, None)
            with sp.Fori(1, PAIRS // 2) as q:
                for p in range(2):
                    load_pair(2 * q + p, p, q)
            sp.wait_ge(y_moved, PAIRS)
            out_of = out.rearrange("(q p s) o -> p (o q) s", p=2, s=NS)
            for p in range(2):
                sp.dma_start(out_of[p:p + 1], y[p * QUAD:p * QUAD + 1]).then_inc(out_written, DMA)
            sp.wait_ge(out_written, 2 * DMA)

        @block.gpsimd
        def _(pool):
            nc.gpsimd.memset(ident[:], 0.0).then_inc(ident_zeroed, 1)
            pool.wait_ge(ident_zeroed, 1)
            nc.gpsimd.affine_select(out=ident[:], in_=ident[:], compare_op=ALU.not_equal, fill=1.0,
                                    base=0, pattern=[[-1, P]], channel_multiplier=1).then_inc(ident_ready, 1)
            nc.gpsimd.iota(row_id[:], pattern=[[1, M]], base=0, channel_multiplier=M).then_inc(row_id_ready, 1)

            def gather(s):
                for n, f in enumerate(gathered):
                    nc.gpsimd.indirect_dma_start(
                        out=rows[:, s, n, :], out_offset=None, in_=table[f],
                        in_offset=bass.IndirectOffsetOnAxis(ap=ids_sb[:, s, f:f + 1], axis=0),
                    ).then_inc(rows_landed[s], DMA)

            for s in range(SLOTS):
                if s == 2:
                    pool.wait_ge(w1_lo_ready, 1)
                pool.wait_ge(ids_landed[s], DMA)
                gather(s)
            with pool.Fori(1, PAIRS // 2) as q:
                for s in range(SLOTS):
                    pool.wait_ge(ids_landed[s], (q + 1) * DMA)
                    b, no = fill_no(s // 2, f"transpose {s % 2}", CHUNKS - 1)
                    pool.wait_ge(filled[b], (q - 1) * FILLS + (no + 1))
                    pool.sem_inc(gathers_begun, 1)
                    gather(s)

        @block.scalar
        def _(act):
            def copy(out_ap, in_ap):
                return nc.scalar.activation(out_ap, in_ap, ACT.Copy)

            def relu1(q, p, b):
                act.wait_ge(layer1_ready, (2 * q + p) * 2 + (b + 1))
                for c in (2 * b, 2 * b + 1):
                    last = nc.scalar.activation(h1[:, c, :], mlp_ps[b][:, c % 2, :], ACT.Relu, bias=bias1[:, c:c + 1])
                last.then_inc(h1_ready, 1)

            def relu2(q, p):
                act.wait_ge(layer2_ready, 2 * q + (p + 1))
                for m in range(C2):
                    last = nc.scalar.activation(h2[:, m, :], mlp_ps[m][:, 0, :], ACT.Relu, bias=bias2[:, m:m + 1])
                last.then_inc(h2_ready, 1)

            def split(q, p, h):
                for e in range(2):
                    act.wait_ge(dots_moved[e], (2 * q + p) * (TILES * UNITS) + ((h + 1) * UNITS))
                tile = slice(h * P, (h + 1) * P)
                copy(dots_hi[:, :, tile], dots[:, :, tile]).then_inc(split_hi, 1)

            def pair(q, p, first=False, last=False):
                for kind, n in STEPS:
                    if (kind, n) in fills:
                        b, no = fill_no(p, kind, n)
                        if b == 1:
                            act.wait_ge(filled[1], q * FILLS + (no + 1))
                            move_fill(copy, 1, kind, n).then_inc(moved[1], 1)
                    elif kind == "gram":
                        act.wait_ge(gram_ready, (2 * q + p) * (TILES * UNITS) + (n + 1))
                        move_dots(copy, DOT_BLOCKS[1], n // UNITS, n % UNITS).then_inc(dots_moved[1], 1)
                    elif (kind, n) == ("split", 0):
                        split(q, p, 0)
                    elif (kind, n) == ("split", 1) and not first:
                        split(*before(q, p), 1)
                    elif kind == "layer 1" and n % 2 and not first:
                        relu1(*before(q, p), n // 2)
                    elif (kind, n) == ("layer 2", C2 - 1) and not first:
                        relu2(*before(q, p))
                    if first and (kind, n) == SPLIT_WEIGHTS_AFTER:
                        act.wait_ge(w1_summed, 1)
                        copy(w1_hi[:], w1[:, 0:KT + 1, :]).then_inc(w1_hi_ready, 1)

            for x in range(X):
                act.wait_ge(table_landed[x % 2], (x // 2 + 1) * DMA)
                copy(table_hi[:, x].rearrange("p m d -> p (m d)"), staging[x % 2]).then_inc(table_hi_ready, 1)
            run_pairs(act, pair)
            split(PAIRS // 2 - 1, 1, 1)
            for b in range(2):
                relu1(PAIRS // 2 - 1, 1, b)
            relu2(PAIRS // 2 - 1, 1)

        @block.vector
        def _(dve):
            def build_onehot(q, p, x):
                if x >= 2:
                    b, no = fill_no(p, "look up", x - 2)
                    dve.wait_ge(filled[b], q * FILLS + (no + 1))
                nc.vector.tensor_tensor(
                    onehot[:, x % 2], ids_wide[:, x, :].unsqueeze(1).to_broadcast([TP, M, NS]),
                    row_id[:].unsqueeze(2).to_broadcast([TP, M, NS]), ALU.is_equal).then_inc(onehot_ready, 1)

            def move_y(q, p):
                dve.wait_ge(y_ps_ready, 2 * q + (p + 1))
                to = y[p * QUAD:p * QUAD + 1, q, :] if isinstance(q, int) else \
                    y[p * QUAD:p * QUAD + 1, bass.ds(q, 1), :].rearrange("o q s -> o (q s)")
                nc.vector.tensor_scalar(to, mlp_ps[1][0:1, 1, :], 1.0, None, ALU.mult).then_inc(y_moved, 1)

            def split(q, p, h):
                dve.wait_ge(split_hi, (2 * q + p) * TILES + (h + 1))
                tile = slice(h * P, (h + 1) * P)
                nc.vector.tensor_tensor(dots_lo[:, :, tile], dots[:, :, tile], dots_hi[:, :, tile].bitcast(fp32),
                                        ALU.subtract).then_inc(split_lo, 1)

            def pair(q, p, first=False, last=False):
                for kind, n in STEPS:
                    if (kind, n) in fills:
                        b, no = fill_no(p, kind, n)
                        if b == 0:
                            dve.wait_ge(filled[0], q * FILLS + (no + 1))
                            move_fill(nc.vector.tensor_copy, 0, kind, n).then_inc(moved[0], 1)
                    elif kind == "gram":
                        dve.wait_ge(gram_ready, (2 * q + p) * (TILES * UNITS) + (n + 1))
                        move_dots(nc.vector.tensor_copy, DOT_BLOCKS[0], n // UNITS, n % UNITS).then_inc(dots_moved[0], 1)
                    elif (kind, n) == ("split", 0):
                        split(q, p, 0)
                    elif (kind, n) == ("split", 1) and not first:
                        split(*before(q, p), 1)
                    elif kind == "layer 3" and not first:
                        move_y(*before(q, p))
                    if kind == "look up" and n + 2 < X:
                        build_onehot(q, p, n + 2)
                    if first and (kind, n) == SPLIT_WEIGHTS_AFTER:
                        dve.wait_ge(weights_landed, WEIGHT_DMAS * DMA)
                        nc.vector.tensor_tensor(w1[:, KT, :], w1[:, KT, :], w1[:, KT + 1, :], ALU.add).then_inc(w1_summed, 1)
                        dve.wait_ge(w1_hi_ready, 1)
                        nc.vector.tensor_tensor(w1_lo[:], w1[:, 0:KT + 1, :], w1_hi[:].bitcast(fp32),
                                                ALU.subtract).then_inc(w1_lo_ready, 1)
                    if (kind, n) in BUILD_AHEAD and not last:
                        if BUILD_AHEAD[kind, n] == 0:
                            dve.wait_ge(ids_wide_landed, (2 * q + (p + 2)) * DMA)
                        build_onehot(*after(q, p), BUILD_AHEAD[kind, n])

            nc.vector.memset(w1[:, 0:KT, :], 0.0).then_inc(w1_zeroed, 1)
            nc.vector.memset(vecs[:, :, V:QUAD], 0.0).then_inc(pads_zeroed, 1)
            for x in range(X):
                dve.wait_ge(table_hi_ready, x + 1)
                nc.vector.tensor_tensor(table_lo[:, x].rearrange("p m d -> p (m d)"), staging[x % 2],
                                        table_hi[:, x].rearrange("p m d -> p (m d)").bitcast(fp32),
                                        ALU.subtract).then_inc(table_lo_ready, 1)
            dve.wait_ge(table_lo_ready, X)
            nc.vector.memset(dots[last_rows:P, KT - 1, :], 0.0).then_inc(dots_padded, 1)
            dve.wait_ge(row_id_ready, 1)
            dve.wait_ge(ids_wide_landed, DMA)
            for x in range(2):
                build_onehot(0, 0, x)
            run_pairs(dve, pair)
            split(PAIRS // 2 - 1, 1, 1)
            move_y(PAIRS // 2 - 1, 1)

        @block.tensor
        def _(pe):
            def wait_bank(q, p, b, no):
                if not (isinstance(q, int) and q == 0 and no == 0):
                    pe.wait_ge(moved[b], q * FILLS + no)

            def look_up(q, p, x, first):
                b, no = fill_no(p, "look up", x)
                if first:
                    pe.wait_ge(table_lo_ready, x + 1)
                pe.wait_ge(onehot_ready, (2 * q + p) * X + (x + 1))
                wait_bank(q, p, b, no)
                for m in range(M):
                    for part in (table_hi, table_lo):
                        last = nc.tensor.matmul(looked_up[b], part[:, x, m, :], onehot[:, x % 2, m, :],
                                                start=(m == 0 and part is table_hi), stop=(m == M - 1 and part is table_lo))
                last.then_inc(filled[b], 1)

            def transpose(q, p, h, n):
                b, no = fill_no(p, f"transpose {h}", n)
                s = 2 * p + h
                if n == 0:
                    pe.wait_ge(rows_landed[s], (q + 1) * (G * DMA))
                    pe.wait_ge(dense_landed[h], (2 * q + (p + 1)) * DMA)
                wait_bank(q, p, b, no)
                for at, v in enumerate(CHUNK_VECTORS[n]):
                    source = dense_rows[:, h, :] if v == F else rows[:, s, gathered.index(v), :]
                    last = nc.tensor.transpose(fill_ps[b][:, at, :], source, ident[:])
                last.then_inc(filled[b], 1)

            def gram(q, p, n, first):
                h, u = n // UNITS, n % UNITS
                if u == 0:
                    for b in range(2):
                        pe.wait_ge(moved[b], q * FILLS + (last_fill(p, h, b) + 1))
                if not (first and n == 0):
                    for e in range(2):
                        pe.wait_ge(dots_moved[e], (2 * q + p) * (TILES * UNITS) + n)
                for g in range(GROUPS_PER_UNIT):
                    at = h * P + (u * GROUPS_PER_UNIT + g) * GROUP
                    last = nc.tensor.matmul(gram_ps[:, g, 0:GROUP * F].rearrange("p (s g) -> p s g", s=GROUP),
                                            vecs[:, at:at + GROUP, :].rearrange("d s v -> d (s v)"),
                                            vecs[:, at:at + GROUP, 0:F], start=True, stop=True)
                last.then_inc(gram_ready, 1)

            def layer1(q, p, c):
                if c == 0:
                    pe.wait_ge(split_lo, (2 * q + (p + 1)) * TILES)
                to, cols = mlp_ps[c // 2][:, c % 2, :], slice(c * P, (c + 1) * P)
                for k in range(KT + 1):
                    for turn, (a, b) in enumerate(((w1_hi, dots_hi), (w1_hi, dots_lo), (w1_lo, dots_hi))):
                        last = nc.tensor.matmul(to, a[:, k, cols], b[:, k, :], start=(k == turn == 0), stop=(k == KT and turn == 2))
                if c % 2:
                    last.then_inc(layer1_ready, 1)

            def layer2(q, p, m):
                if m == 0:
                    pe.wait_ge(h1_ready, (2 * q + p) * 2 + 2)
                for c in range(C1):
                    last = nc.tensor.matmul(mlp_ps[m][:, 0, :], w2[:, c, m * P:(m + 1) * P], h1[:, c, :],
                                            start=(c == 0), stop=(c == C1 - 1))
                if m == C2 - 1:
                    last.then_inc(layer2_ready, 1)

            def layer3(q, p):
                pe.wait_ge(h2_ready, 2 * q + (p + 1))
                for m in range(C2):
                    last = nc.tensor.matmul(mlp_ps[1][0:1, 1, :], w3[:, m:m + 1], h2[:, m, :],
                                            start=(m == 0), stop=(m == C2 - 1))
                last.then_inc(y_ps_ready, 1)

            def pair(q, p, first=False, last=False):
                for kind, n in STEPS:
                    if kind == "look up":
                        look_up(q, p, n, first)
                    elif kind in ("transpose 0", "transpose 1"):
                        transpose(q, p, int(kind[-1]), n)
                    elif kind == "gram":
                        gram(q, p, n, first)
                    elif kind == "layer 1" and not first:
                        layer1(*before(q, p), n)
                    elif kind == "layer 2" and not first:
                        layer2(*before(q, p), n)
                    elif kind == "layer 3" and not first:
                        layer3(*before(q, p))

            pe.wait_ge(ident_ready, 1)
            pe.wait_ge(pads_zeroed, 1)
            pe.wait_ge(dots_padded, 1)
            run_pairs(pe, pair)
            pe.wait_ge(y_moved, PAIRS - 1)
            for c in range(C1):
                layer1(PAIRS // 2 - 1, 1, c)
            for m in range(C2):
                layer2(PAIRS // 2 - 1, 1, m)
            layer3(PAIRS // 2 - 1, 1)


def kernel(**inputs):
    import concourse.bacc as bacc
    from concourse.bass_utils import run_bass_kernel_spmd

    nc = bacc.Bacc("TRN2", target_bir_lowering=False, num_devices=1)
    inputs["ids_t"] = np.asarray(inputs["ids"]).T[list(ON_CHIP)]
    arrays, aps = {}, {}
    for name, a in inputs.items():
        a = np.ascontiguousarray(a)
        arrays[f"in_{name}"] = a
        aps[name] = nc.dram_tensor(f"in_{name}", a.shape, mybir.dt.from_np(a.dtype), kind="ExternalInput").ap()
    B, F = inputs["ids"].shape
    out = nc.dram_tensor("out_y", (B, 1), mybir.dt.float32, kind="ExternalOutput").ap()
    dlrm_tower(nc, [aps[f"tbl_{f}"] for f in range(F)], aps["r_dense_features"], aps["ids"], aps["ids_t"],
               aps["W_top1"], aps["b_top1"], aps["W_top2"], aps["b_top2"], aps["W_top3"], out)
    return run_bass_kernel_spmd(nc, [arrays], core_ids=[0]).results[0]["out_y"]
```

```python
from contextlib import ExitStack

import numpy as np

import concourse.bass as bass
from concourse import mybir

P = 128
QUAD = 32
TILES = 2
CHUNK = 4
GROUP = 4
GROUPS_PER_UNIT = 16
ROWS_AT_MOST = 1024
SLOTS = 4
ON_CHIP = (12, 14, 15, 16, 24, 25)
ONEHOTS = 3
DMA = 16
CHUNK_VECTORS = [[0, 1, 2, 3], [4, 5, 6, 7], [8, 9, 10, 11], [17, 18, 19, 20], [21, 22, 23], [13, 26]]
STEPS = [("build", 5), ("look up", 3), ("place", 3), ("layer 1", 0), ("layer 1", 1), ("look up", 4), ("place", 4),
         ("look up", 5), ("place", 5), ("transpose 0", 0), ("transpose 0", 1), ("layer 1", 2), ("transpose 0", 2),
         ("transpose 0", 3), ("layer 1", 3), ("transpose 0", 4), ("transpose 0", 5), ("layer 1", 4),
         ("transpose 1", 0), ("transpose 1", 1), ("build next", 0), ("gram", 0), ("layer 1", 5), ("layer 1", 6),
         ("layer 1", 7), ("transpose 1", 2), ("transpose 1", 3), ("build next", 1), ("gram", 1),
         ("transpose 1", 4), ("transpose 1", 5), ("split", 0), ("build next", 2), ("layer 2", 0), ("layer 2", 1),
         ("layer 2", 2), ("gram", 2), ("look up next", 0), ("look up next", 1), ("build next", 3),
         ("build next", 4), ("place next", 0), ("place next", 1), ("gram", 3), ("layer 2", 3), ("look up next", 2),
         ("place next", 2), ("layer 3", 0), ("split", 1)]
FIRST_STEPS = [("build", 5), ("look up", 3), ("place", 3), ("look up", 4), ("place", 4), ("look up", 5), ("place", 5),
               ("transpose 0", 0), ("transpose 0", 1), ("transpose 0", 2), ("transpose 0", 3), ("transpose 0", 4),
               ("transpose 0", 5), ("transpose 1", 0), ("transpose 1", 1), ("build next", 0), ("gram", 0),
               ("transpose 1", 2), ("transpose 1", 3), ("build next", 1), ("gram", 1), ("transpose 1", 4),
               ("transpose 1", 5), ("split", 0), ("build next", 2), ("gram", 2), ("look up next", 0),
               ("look up next", 1), ("build next", 3), ("build next", 4), ("place next", 0), ("place next", 1),
               ("gram", 3), ("look up next", 2), ("place next", 2), ("split", 1)]
LAST_STEPS = [("build", 5), ("look up", 3), ("place", 3), ("layer 1", 0), ("layer 1", 1), ("look up", 4), ("place", 4),
              ("look up", 5), ("place", 5), ("transpose 0", 0), ("transpose 0", 1), ("layer 1", 2), ("transpose 0", 2),
              ("transpose 0", 3), ("layer 1", 3), ("transpose 0", 4), ("transpose 0", 5), ("transpose 1", 0),
              ("transpose 1", 1), ("gram", 0), ("layer 1", 4), ("layer 1", 5), ("layer 1", 6), ("gram", 1),
              ("layer 1", 7), ("transpose 1", 2), ("transpose 1", 3), ("layer 2", 0), ("layer 2", 1),
              ("transpose 1", 4), ("transpose 1", 5), ("split", 0), ("gram", 2), ("layer 2", 2), ("layer 2", 3),
              ("gram", 3), ("layer 3", 0), ("split", 1)]


def runs_of(vectors):
    runs = []
    for n, v in enumerate(vectors):
        if runs and v == runs[-1][0] + runs[-1][1]:
            runs[-1][1] += 1
        else:
            runs.append([v, 1, n])
    return runs


def dlrm_tower(nc, table, dense, ids, ids_t, w1_rows, partner_rows, b1, W2, b2, W3, out):
    fp32, fp32r, int32 = mybir.dt.float32, mybir.dt.float32r, mybir.dt.int32
    ALU, ACT = mybir.AluOpType, mybir.ActivationFunctionType

    B, F = ids.shape
    D = dense.shape[1]
    N1, N2 = W2.shape
    V = F + 1
    HALF = V // 2
    COLUMNS, PARTNERS = HALF + 1, V - HALF - 1
    KT = -(-COLUMNS // 4)
    last_rows = (COLUMNS - 4 * (KT - 1)) * QUAD
    NS = P * TILES
    PAIRS = B // NS
    UNITS = P // (GROUP * GROUPS_PER_UNIT)
    GRAM_ROWS = P - (QUAD - V)
    C1, C2 = N1 // P, N2 // P
    WEIGHT_DMAS = 4 + KT + 2

    gathers_of = [[f for f in chunk if f != F] for chunk in CHUNK_VECTORS]
    gathered = sum(gathers_of, [])
    G, X = len(gathered), len(ON_CHIP)
    TR = table[ON_CHIP[0]].shape[0]
    M = ROWS_AT_MOST // P
    TP = TR // M
    assert all(table[f].shape[0] == TR for f in ON_CHIP) and TP * M == TR

    CHUNKS = len(CHUNK_VECTORS)
    assert sorted(gathered + [*ON_CHIP]) == list(range(F))
    ahead = [("look up", n) for kind, n in STEPS if kind == "look up next"]
    builds_ahead = sorted(n for kind, n in STEPS if kind == "build next")
    assert len(ahead) == ONEHOTS <= len(builds_ahead)
    placed_ahead = [("place", n) for _, n in ahead]
    fills = ahead + [step for step in STEPS if step[0] in ("look up", "transpose 0", "transpose 1")]
    FILLS = len(fills)
    assert FILLS == X + 2 * CHUNKS

    def fill_no(p, kind, n):
        at = p * FILLS + fills.index(("look up" if kind == "place" else kind, n))
        return at % 2, at // 2

    def last_fill(p, h, b):
        kinds = (f"transpose {h}", "look up")
        return max(fill_no(p, *fill)[1] for fill in fills if fill[0] in kinds and fill_no(p, *fill)[0] == b)

    with ExitStack() as ctx:
        def sb(name, shape, dt=fp32):
            return ctx.enter_context(nc.sbuf_tensor(name, shape, dt))

        def sem(name):
            return ctx.enter_context(nc.semaphore(name))

        ids_sb = sb("ids_sb", [P, SLOTS, F], int32)
        rows = sb("rows", [P, SLOTS, G, D])
        dense_rows = sb("dense_rows", [P, TILES, D])
        ids_wide = sb("ids_wide", [TP, X, NS], int32)
        row_id = sb("row_id", [TP, M], int32)
        onehot = sb("onehot", [TP, ONEHOTS, M, NS], fp32r)
        table_hi = sb("table_hi", [TP, X, M, D], fp32r)
        table_lo = sb("table_lo", [TP, X, M, D], fp32r)
        vecs = sb("vecs", [D, NS, QUAD])
        dots = sb("dots", [P, KT + 1, NS])
        dots_hi = sb("dots_hi", [P, KT + 1, NS], fp32r)
        dots_lo = sb("dots_lo", [P, KT + 1, NS], fp32r)
        h1 = sb("h1", [P, C1, NS])
        h2 = sb("h2", [P, C2, NS])
        y = sb("y", [QUAD + 1, PAIRS // 2, NS])
        w1_hi = sb("w1_hi", [P, KT + 1, N1], fp32r)
        w1_lo = sb("w1_lo", [P, KT + 1, N1], fp32r)
        w2 = sb("w2", [P, C1, N2])
        w3 = sb("w3", [P, C2])
        bias1 = sb("bias1", [P, C1])
        bias2 = sb("bias2", [P, C2])
        ident = sb("ident", [P, P])
        staging = [vecs[0:TP].rearrange("p s v -> p (s v)")[:, x * M * D:(x + 1) * M * D] for x in range(X)]
        partner = sb("partner", [P, 4, KT], int32)
        w1_spare = sb("w1_spare", [P, N1])
        w1 = [place[:].rearrange("p k n -> p (k n)")[:, k * N1:(k + 1) * N1]
              for place, tiles in ((dots, 2), (h1, 2), (h2, 1)) for k in range(tiles)] + [w1_spare[:]]
        assert len(w1) == KT + 2

        fill_ps = [ctx.enter_context(nc.psum_tensor(f"fill_ps{b}", [P, CHUNK, P], fp32)) for b in range(2)]
        gram_ps = ctx.enter_context(nc.psum_tensor("gram_ps", [P, GROUPS_PER_UNIT, P], fp32))
        mlp_ps = [ctx.enter_context(nc.psum_tensor(f"mlp_ps{b}", [P, 2, NS], fp32)) for b in range(2)]
        looked_up = [fill_ps[b][:].rearrange("d v s -> d (v s)")[:, 0:NS] for b in range(2)]

        ids_landed = [sem(f"ids_landed{s}") for s in range(SLOTS)]
        dense_landed = [sem(f"dense_landed{h}") for h in range(TILES)]
        rows_landed = [[sem(f"rows_landed{s}_{n}") for n in range(CHUNKS)] for s in range(SLOTS)]
        gathers_begun = sem("gathers_begun")
        ids_wide_landed = sem("ids_wide_landed")
        table_landed = [sem(f"table_landed{x}") for x in range(X)]
        table_hi_ready = sem("table_hi_ready")
        table_lo_ready = sem("table_lo_ready")
        weights_landed = sem("weights_landed")
        partner_landed = sem("partner_landed")
        w1_summed = sem("w1_summed")
        w1_hi_ready = sem("w1_hi_ready")
        w1_lo_ready = sem("w1_lo_ready")
        ident_zeroed = sem("ident_zeroed")
        ident_ready = sem("ident_ready")
        row_id_ready = sem("row_id_ready")
        pads_zeroed = sem("pads_zeroed")
        onehot_ready = sem("onehot_ready")
        filled = [sem(f"filled{b}") for b in range(2)]
        moved = [sem(f"moved{b}") for b in range(2)]
        gram_ready = sem("gram_ready")
        columns_moved = sem("columns_moved")
        partners_begun = sem("partners_begun")
        dots_moved = sem("dots_moved")
        split_hi = sem("split_hi")
        split_lo = sem("split_lo")
        dots_padded = sem("dots_padded")
        layer1_ready = sem("layer1_ready")
        h1_ready = sem("h1_ready")
        layer2_ready = sem("layer2_ready")
        h2_ready = sem("h2_ready")
        y_ps_ready = sem("y_ps_ready")
        y_moved = sem("y_moved")
        out_written = sem("out_written")

        ids_of = ids.rearrange("(q s p) f -> q s p f", s=SLOTS, p=P)
        dense_of = dense.rearrange("(i h p) d -> i h p d", h=TILES, p=P)

        def run_pairs(engine, pair):
            pair(0, 0, first=True)
            with engine.Fori(0, PAIRS // 2 - 1) as q:
                pair(q, 1)
                pair(q + 1, 0)
            pair(PAIRS // 2 - 1, 1, last=True)

        def before(q, p):
            return (q, 0) if p else (q - 1, 1)

        def after(q, p):
            return (q + 1, 0) if p else (q, 1)

        def is_first(q, p):
            return isinstance(q, int) and (q, p) == (0, 0)

        def steps(q, p, first, last):
            for kind, n in FIRST_STEPS if first else LAST_STEPS if last else STEPS:
                if kind.startswith("layer"):
                    if not first:
                        yield kind, n, *before(q, p)
                elif kind.endswith("next"):
                    if not last:
                        yield kind[:-5], n, *after(q, p)
                else:
                    yield kind, n, q, p

        def move_fill(copy, b, kind, n):
            if kind == "place":
                return copy(vecs[:, :, ON_CHIP[n]], looked_up[b])
            h = int(kind[-1])
            for f, m, at in runs_of(CHUNK_VECTORS[n]):
                last = copy(vecs[:, h * P:(h + 1) * P, f:f + m].rearrange("d s v -> d v s"), fill_ps[b][:, at:at + m, :])
                if f + m == V:
                    last = copy(dots[:, KT, h * P:(h + 1) * P], fill_ps[b][:, at + m - 1, :])
            return last

        def dots_of_block(n, block, columns, shift):
            at = n * GROUP * GROUPS_PER_UNIT + block
            for r in range(4):
                m = len(range(r, columns, 4))
                yield (r, dots[r * QUAD:(r + 1) * QUAD, 0:m, at:at + GROUP * (GROUPS_PER_UNIT - 1) + 1:GROUP]
                       .rearrange("f k g -> f g k"),
                       gram_ps[block * QUAD:(block + 1) * QUAD, :, block * V + shift + r:block * V + shift + columns:4])

        block = ctx.enter_context(nc.Block())

        @block.sync
        def _(sp):
            for s in range(SLOTS):
                sp.dma_start(ids_sb[:, s, :], ids_of[0, s]).then_inc(ids_landed[s], DMA)
                if s < TILES:
                    sp.dma_start(dense_rows[:, s, :], dense_of[0, s]).then_inc(dense_landed[s], DMA)
                if s < 2:
                    sp.dma_start(staging[s], table[ON_CHIP[s]].rearrange("(p m) d -> p (m d)", m=M)).then_inc(table_landed[s], DMA)
            sp.dma_start(ids_wide[:], ids_t[:, 0:NS].partition_broadcast(TP)).then_inc(ids_wide_landed, DMA)
            for x in range(2, X):
                sp.dma_start(staging[x], table[ON_CHIP[x]].rearrange("(p m) d -> p (m d)", m=M)).then_inc(table_landed[x], DMA)

            sp.dma_start(partner[:], partner_rows).then_inc(partner_landed, DMA)
            for k in range(KT + 2):
                sp.dma_start(w1[k], w1_rows[k]).then_inc(weights_landed, DMA)
            sp.dma_start(w2[:], W2.rearrange("(c p) n -> p c n", p=P)).then_inc(weights_landed, DMA)
            sp.dma_start(w3[:], W3.rearrange("(c p) o -> p (c o)", p=P), allow_slow_non_contiguous=True).then_inc(weights_landed, DMA)
            sp.dma_start(bias1[:], b1.rearrange("(c p) -> p c", p=P), allow_slow_non_contiguous=True).then_inc(weights_landed, DMA)
            sp.dma_start(bias2[:], b2.rearrange("(c p) -> p c", p=P), allow_slow_non_contiguous=True).then_inc(weights_landed, DMA)

            def load_pair(i, p, q_of_slots):
                if q_of_slots is not None:
                    for s in (2 * p, 2 * p + 1):
                        b, no = fill_no(p, f"transpose {s % 2}", CHUNKS - 1)
                        sp.wait_ge(filled[b], (q_of_slots - 1) * FILLS + (no + 1))
                        sp.dma_start(ids_sb[:, s, :], ids_of[bass.ds(q_of_slots, 1), s].rearrange("o p f -> (o p) f")).then_inc(ids_landed[s], DMA)
                sp.wait_ge(onehot_ready, i * X)
                cols = ids_t[:, i * NS:(i + 1) * NS] if isinstance(i, int) else ids_t[:, bass.ds(i * NS, NS)]
                sp.dma_start(ids_wide[:], cols.partition_broadcast(TP)).then_inc(ids_wide_landed, DMA)
                for h in range(TILES):
                    (q, pp) = (0, 0) if isinstance(i, int) else before(q_of_slots, p)
                    b, no = fill_no(pp, f"transpose {h}", CHUNKS - 1)
                    sp.wait_ge(filled[b], q * FILLS + (no + 1))
                    tile = dense_of[i, h] if isinstance(i, int) else dense_of[bass.ds(i, 1), h].rearrange("o p d -> (o p) d")
                    sp.dma_start(dense_rows[:, h, :], tile).then_inc(dense_landed[h], DMA)

            load_pair(1, 1, None)
            with sp.Fori(1, PAIRS // 2) as q:
                for p in range(2):
                    load_pair(2 * q + p, p, q)
            sp.wait_ge(y_moved, PAIRS)
            out_of = out.rearrange("(q p s) o -> p (o q) s", p=2, s=NS)
            for p in range(2):
                sp.dma_start(out_of[p:p + 1], y[p * QUAD:p * QUAD + 1]).then_inc(out_written, DMA)
            sp.wait_ge(out_written, 2 * DMA)

        @block.gpsimd
        def _(pool):
            nc.gpsimd.memset(ident[:], 0.0).then_inc(ident_zeroed, 1)
            pool.wait_ge(ident_zeroed, 1)
            nc.gpsimd.affine_select(out=ident[:], in_=ident[:], compare_op=ALU.not_equal, fill=1.0,
                                    base=0, pattern=[[-1, P]], channel_multiplier=1).then_inc(ident_ready, 1)
            nc.gpsimd.iota(row_id[:], pattern=[[1, M]], base=0, channel_multiplier=M).then_inc(row_id_ready, 1)

            def gather(s):
                for n in range(CHUNKS):
                    for f in gathers_of[n]:
                        nc.gpsimd.indirect_dma_start(
                            out=rows[:, s, gathered.index(f), :], out_offset=None, in_=table[f],
                            in_offset=bass.IndirectOffsetOnAxis(ap=ids_sb[:, s, f:f + 1], axis=0),
                        ).then_inc(rows_landed[s][n], DMA)

            for s in range(SLOTS):
                pool.wait_ge(ids_landed[s], DMA)
                gather(s)
            with pool.Fori(1, PAIRS // 2) as q:
                for s in range(SLOTS):
                    pool.wait_ge(ids_landed[s], (q + 1) * DMA)
                    b, no = fill_no(s // 2, f"transpose {s % 2}", CHUNKS - 1)
                    pool.wait_ge(filled[b], (q - 1) * FILLS + (no + 1))
                    pool.sem_inc(gathers_begun, 1)
                    gather(s)

        @block.scalar
        def _(act):
            def copy(out_ap, in_ap):
                return nc.scalar.activation(out_ap, in_ap, ACT.Copy)

            def relu1(q, p, b):
                act.wait_ge(layer1_ready, (2 * q + p) * 2 + (b + 1))
                for c in (2 * b, 2 * b + 1):
                    last = nc.scalar.activation(h1[:, c, :], mlp_ps[b][:, c % 2, :], ACT.Relu, bias=bias1[:, c:c + 1])
                last.then_inc(h1_ready, 1)

            def relu2(q, p, m):
                act.wait_ge(layer2_ready, (2 * q + p) * C2 + (m + 1))
                nc.scalar.activation(h2[:, m, :], mlp_ps[m][:, 0, :], ACT.Relu, bias=bias2[:, m:m + 1]).then_inc(h2_ready, 1)

            def split(q, p, h):
                act.wait_ge(dots_moved, (2 * q + p) * (TILES * UNITS) + ((h + 1) * UNITS))
                tile = slice(h * P, (h + 1) * P)
                copy(dots_hi[:, :, tile], dots[:, :, tile]).then_inc(split_hi, 1)

            def place(q, p, kind, n):
                b, no = fill_no(p, kind, n)
                if b == 1:
                    act.wait_ge(filled[1], q * FILLS + (no + 1))
                    if (kind, n) in placed_ahead and not is_first(q, p):
                        act.wait_ge(gram_ready, (2 * q + p) * (TILES * UNITS))
                    move_fill(copy, 1, kind, n).then_inc(moved[1], 1)

            def pair(i, h, first=False, last=False):
                for kind, n, q, p in steps(i, h, first, last):
                    if kind.startswith("transpose") or kind == "place":
                        place(q, p, kind, n)
                    elif kind == "gram":
                        act.wait_ge(gram_ready, (2 * q + p) * (TILES * UNITS) + (n + 1))
                        for block in range(GROUP):
                            for _, to, products in dots_of_block(n, block, COLUMNS, 0):
                                last_copy = copy(to, products)
                            last_copy.then_inc(columns_moved, 1)
                    elif kind == "split":
                        split(q, p, n)
                    elif kind == "layer 1" and n % 4 == 3:
                        relu1(q, p, n // 4)
                    elif kind == "layer 2" and n % 2:
                        relu2(q, p, n // 2)

            for x in range(X):
                act.wait_ge(table_landed[x], DMA)
                copy(table_hi[:, x].rearrange("p m d -> p (m d)"), staging[x]).then_inc(table_hi_ready, 1)
            act.wait_ge(table_lo_ready, X)
            for _, n in ahead[:2]:
                place(0, 0, "place", n)
            act.wait_ge(w1_summed, 1)
            for k in range(KT + 1):
                copy(w1_hi[:, k], w1[k]).then_inc(w1_hi_ready, 1)
            for _, n in ahead[2:]:
                place(0, 0, "place", n)
            run_pairs(act, pair)
            for b in range(2):
                relu1(PAIRS // 2 - 1, 1, b)
            for m in range(C2):
                relu2(PAIRS // 2 - 1, 1, m)

        @block.vector
        def _(dve):
            def build_onehot(q, p, x):
                if x >= ONEHOTS:
                    b, no = fill_no(p, "look up", x - ONEHOTS)
                    dve.wait_ge(filled[b], q * FILLS + (no + 1))
                nc.vector.tensor_tensor(
                    onehot[:, x % ONEHOTS], ids_wide[:, x, :].unsqueeze(1).to_broadcast([TP, M, NS]),
                    row_id[:].unsqueeze(2).to_broadcast([TP, M, NS]), ALU.is_equal).then_inc(onehot_ready, 1)

            def move_y(q, p):
                dve.wait_ge(y_ps_ready, 2 * q + (p + 1))
                to = y[p * QUAD:p * QUAD + 1, q, :] if isinstance(q, int) else \
                    y[p * QUAD:p * QUAD + 1, bass.ds(q, 1), :].rearrange("o q s -> o (q s)")
                nc.vector.tensor_scalar(to, mlp_ps[1][0:1, 1, :], 1.0, None, ALU.mult).then_inc(y_moved, 1)

            def split(q, p, h):
                dve.wait_ge(split_hi, (2 * q + p) * TILES + (h + 1))
                tile = slice(h * P, (h + 1) * P)
                nc.vector.tensor_tensor(dots_lo[:, :, tile], dots[:, :, tile], dots_hi[:, :, tile].bitcast(fp32),
                                        ALU.subtract).then_inc(split_lo, 1)

            def place(q, p, kind, n):
                b, no = fill_no(p, kind, n)
                if b == 0:
                    dve.wait_ge(filled[0], q * FILLS + (no + 1))
                    if (kind, n) in placed_ahead and not is_first(q, p):
                        dve.wait_ge(gram_ready, (2 * q + p) * (TILES * UNITS))
                    move_fill(nc.vector.tensor_copy, 0, kind, n).then_inc(moved[0], 1)

            def pair(i, h, first=False, last=False):
                for kind, n, q, p in steps(i, h, first, last):
                    if kind.startswith("transpose") or kind == "place":
                        place(q, p, kind, n)
                    elif kind == "gram":
                        for block in range(GROUP):
                            dve.wait_ge(columns_moved, (2 * q + p) * (TILES * UNITS * GROUP) + (n * GROUP + block + 1))
                            dve.sem_inc(partners_begun, 1)
                            for r, to, products in dots_of_block(n, block, PARTNERS, COLUMNS):
                                rows_of = partner[block * QUAD:(block + 1) * QUAD, r, 0:to.shape[2]]
                                last_copy = nc.vector.copy_predicated(
                                    to, rows_of.unsqueeze(1).to_broadcast([QUAD, GROUPS_PER_UNIT, to.shape[2]]), products)
                        last_copy.then_inc(dots_moved, 1)
                    elif kind == "split":
                        split(q, p, n)
                    elif kind == "layer 3":
                        move_y(q, p)
                    elif kind == "build":
                        if n == 0:
                            dve.wait_ge(ids_wide_landed, (2 * q + (p + 1)) * DMA)
                        build_onehot(q, p, n)

            nc.vector.memset(gram_ps[P - QUAD:P], 0.0)
            for x in range(X):
                dve.wait_ge(table_hi_ready, x + 1)
                nc.vector.tensor_tensor(table_lo[:, x].rearrange("p m d -> p (m d)"), staging[x],
                                        table_hi[:, x].rearrange("p m d -> p (m d)").bitcast(fp32),
                                        ALU.subtract).then_inc(table_lo_ready, 1)
                if 1 <= x <= ONEHOTS:
                    if x == 1:
                        dve.wait_ge(row_id_ready, 1)
                        dve.wait_ge(ids_wide_landed, DMA)
                    build_onehot(0, 0, x - 1)
            dve.wait_ge(table_lo_ready, X)
            for _, n in ahead[:2]:
                place(0, 0, "place", n)
            nc.vector.memset(vecs[:, :, V:QUAD], 0.0).then_inc(pads_zeroed, 1)
            dve.wait_ge(weights_landed, WEIGHT_DMAS * DMA)
            nc.vector.tensor_tensor(w1[KT], w1[KT], w1[KT + 1], ALU.add).then_inc(w1_summed, 1)
            for k in range(KT + 1):
                dve.wait_ge(w1_hi_ready, k + 1)
                nc.vector.tensor_tensor(w1_lo[:, k], w1[k], w1_hi[:, k].bitcast(fp32),
                                        ALU.subtract).then_inc(w1_lo_ready, 1)
            dve.wait_ge(w1_lo_ready, KT + 1)
            nc.vector.memset(dots[last_rows:P, KT - 1, :], 0.0).then_inc(dots_padded, 1)
            for _, n in ahead[2:]:
                place(0, 0, "place", n)
            for n in builds_ahead[ONEHOTS:]:
                build_onehot(0, 0, n)
            dve.wait_ge(partner_landed, DMA)
            run_pairs(dve, pair)
            move_y(PAIRS // 2 - 1, 1)

        @block.tensor
        def _(pe):
            def wait_bank(q, p, b, no):
                if not (isinstance(q, int) and q == 0 and no == 0):
                    pe.wait_ge(moved[b], q * FILLS + no)

            def look_up(q, p, x, first):
                b, no = fill_no(p, "look up", x)
                if first:
                    pe.wait_ge(table_lo_ready, x + 1)
                pe.wait_ge(onehot_ready, (2 * q + p) * X + (x + 1))
                wait_bank(q, p, b, no)
                for m in range(M):
                    for part in (table_hi, table_lo):
                        last = nc.tensor.matmul(looked_up[b], part[:, x, m, :], onehot[:, x % ONEHOTS, m, :],
                                                start=(m == 0 and part is table_hi), stop=(m == M - 1 and part is table_lo))
                last.then_inc(filled[b], 1)

            def transpose(q, p, h, n):
                b, no = fill_no(p, f"transpose {h}", n)
                s = 2 * p + h
                pe.wait_ge(rows_landed[s][n], (q + 1) * (len(gathers_of[n]) * DMA))
                if F in CHUNK_VECTORS[n]:
                    pe.wait_ge(dense_landed[h], (2 * q + (p + 1)) * DMA)
                wait_bank(q, p, b, no)
                for at, v in enumerate(CHUNK_VECTORS[n]):
                    source = dense_rows[:, h, :] if v == F else rows[:, s, gathered.index(v), :]
                    last = nc.tensor.transpose(fill_ps[b][:, at, :], source, ident[:])
                last.then_inc(filled[b], 1)

            def gram(q, p, n, first):
                h, u = n // UNITS, n % UNITS
                if first and n == 0:
                    pe.wait_ge(pads_zeroed, 1)
                    pe.wait_ge(dots_padded, 1)
                if u == 0:
                    for b in range(2):
                        pe.wait_ge(moved[b], q * FILLS + (last_fill(p, h, b) + 1))
                if not (first and n == 0):
                    pe.wait_ge(dots_moved, (2 * q + p) * (TILES * UNITS) + n)
                for g in range(GROUPS_PER_UNIT):
                    at = h * P + (u * GROUPS_PER_UNIT + g) * GROUP
                    last = nc.tensor.matmul(gram_ps[0:GRAM_ROWS, g, 0:GROUP * V].rearrange("p (s g) -> p s g", s=GROUP),
                                            vecs[:, at:at + GROUP, :].rearrange("d s v -> d (s v)")[:, 0:GRAM_ROWS],
                                            vecs[:, at:at + GROUP, 0:V], start=True, stop=True)
                last.then_inc(gram_ready, 1)

            products = [(w, dots_hi, k) for w in (w1_hi, w1_lo) for k in range(KT + 1)] + [(w1_hi, dots_lo, k) for k in range(KT + 1)]

            def layer1(q, p, n):
                if n == 0:
                    pe.wait_ge(split_hi, (2 * q + (p + 1)) * TILES)
                if n == 1:
                    pe.wait_ge(split_lo, (2 * q + (p + 1)) * TILES)
                c, half = n // 2, len(products) // 2
                for w, d, k in products[half:] if n % 2 else products[:half]:
                    last = nc.tensor.matmul(mlp_ps[c // 2][:, c % 2, :], w[:, k, c * P:(c + 1) * P], d[:, k, :],
                                            start=((w, d, k) == products[0]), stop=((w, d, k) == products[-1]))
                if n % 4 == 3:
                    last.then_inc(layer1_ready, 1)

            def layer2(q, p, n):
                if n < 2:
                    pe.wait_ge(h1_ready, (2 * q + p) * 2 + (n + 1))
                m = n // 2
                for c in range(n % 2 * C1 // 2, (n % 2 + 1) * C1 // 2):
                    last = nc.tensor.matmul(mlp_ps[m][:, 0, :], w2[:, c, m * P:(m + 1) * P], h1[:, c, :],
                                            start=(c == 0), stop=(c == C1 - 1))
                if n % 2:
                    last.then_inc(layer2_ready, 1)

            def layer3(q, p):
                pe.wait_ge(h2_ready, (2 * q + p) * C2 + C2)
                for m in range(C2):
                    last = nc.tensor.matmul(mlp_ps[1][0:1, 1, :], w3[:, m:m + 1], h2[:, m, :],
                                            start=(m == 0), stop=(m == C2 - 1))
                last.then_inc(y_ps_ready, 1)

            def pair(i, h, first=False, last=False):
                for kind, n, q, p in steps(i, h, first, last):
                    if kind == "look up":
                        look_up(q, p, n, first)
                    elif kind in ("transpose 0", "transpose 1"):
                        transpose(q, p, int(kind[-1]), n)
                    elif kind == "gram":
                        gram(q, p, n, first)
                    elif kind == "layer 1":
                        layer1(q, p, n)
                    elif kind == "layer 2":
                        layer2(q, p, n)
                    elif kind == "layer 3":
                        layer3(q, p)

            pe.wait_ge(ident_ready, 1)
            for _, n in ahead:
                look_up(0, 0, n, True)
            run_pairs(pe, pair)
            pe.wait_ge(y_moved, PAIRS - 1)
            for n in range(2 * C1):
                layer1(PAIRS // 2 - 1, 1, n)
            for n in range(2 * C2):
                layer2(PAIRS // 2 - 1, 1, n)
            layer3(PAIRS // 2 - 1, 1)


def kernel(**inputs):
    import concourse.bacc as bacc
    from concourse.bass_utils import run_bass_kernel_spmd

    nc = bacc.Bacc("TRN2", target_bir_lowering=False, num_devices=1)
    inputs["ids_t"] = np.asarray(inputs["ids"]).T[list(ON_CHIP)]
    W1 = np.asarray(inputs.pop("W_top1"))
    B, F = inputs["ids"].shape
    D = inputs["r_dense_features"].shape[1]
    half, columns = (F + 1) // 2, (F + 1) // 2 + 1
    k_tiles = -(-columns // 4)
    w1_rows = np.zeros((k_tiles + 2, P, W1.shape[1]), W1.dtype)
    partner_rows = np.zeros((P, 4, k_tiles), np.int32)
    for m in range(columns):
        for f in range(F + 1):
            second = m < f <= m + half and m + columns <= F
            a, b = sorted((f, m + columns if second else m))
            partner_rows[f::QUAD, m % 4, m // 4] = second
            if a != b and (second or (m - f) % (F + 1) <= half):
                row = D + a if b == F else D + F + a * (F - 1) - a * (a - 1) // 2 + b - a - 1
                w1_rows[m // 4, m % 4 * QUAD + f] = W1[row]
    w1_rows[k_tiles], w1_rows[k_tiles + 1] = W1[:D], W1[-D:]
    inputs["w1_rows"], inputs["partner_rows"] = w1_rows, partner_rows
    arrays, aps = {}, {}
    for name, a in inputs.items():
        a = np.ascontiguousarray(a)
        arrays[f"in_{name}"] = a
        aps[name] = nc.dram_tensor(f"in_{name}", a.shape, mybir.dt.from_np(a.dtype), kind="ExternalInput").ap()
    out = nc.dram_tensor("out_y", (B, 1), mybir.dt.float32, kind="ExternalOutput").ap()
    dlrm_tower(nc, [aps[f"tbl_{f}"] for f in range(F)], aps["r_dense_features"], aps["ids"], aps["ids_t"],
               aps["w1_rows"], aps["partner_rows"], aps["b_top1"], aps["W_top2"], aps["b_top2"], aps["W_top3"], out)
    return run_bass_kernel_spmd(nc, [arrays], core_ids=[0]).results[0]["out_y"]
```
